# Optimizing a Trainium2 kernel written in Bass

```python
import numpy as np
import jax
import jax.numpy as jnp

def _softmax(x, axis=-1):
    return jax.nn.softmax(x, axis=axis)

def _gelu(x):
    return jax.nn.gelu(x, approximate=True)

def _silu(x):
    return jax.nn.silu(x)

def _sigmoid(x):
    return jax.nn.sigmoid(x)

def _layernorm(x, axis=-1, eps=1e-05):
    m = jnp.mean(x, axis=axis, keepdims=True)
    v = jnp.var(x, axis=axis, keepdims=True)
    return (x - m) / jnp.sqrt(v + eps)

def _scatter_add(tgt, idx, src, axis=0):
    return tgt.at[idx].add(src)

def _segment_sum(src, seg, n):
    return jax.ops.segment_sum(src, seg, n)
kernel_name = 'mk_flamingo_gated_d1_seqx_r8_f60df6'

def setup_inputs(seed: int=0):
    np.random.seed(seed)
    _w = jnp.asarray

    def _rec_inputs():
        import jax
        import jax.numpy as jnp
        _rk = jax.random.key(seed)
        x = -0.0003929 + 0.9999 * jax.random.normal(jax.random.fold_in(_rk, 1), (16, 100, 128), jnp.float32)
        _lenS = 100 - jax.random.randint(jax.random.fold_in(_rk, 7), (16,), 0, max(1, 100 // 4) + 1, jnp.int32)
        _lenS2 = 1444 - jax.random.randint(jax.random.fold_in(_rk, 8), (16,), 0, max(1, 1444 // 4) + 1, jnp.int32)
        _ctx_1024P = jax.random.normal(jax.random.fold_in(_rk, 11), (16, 16, 128), jnp.float32)
        _ctx_1024c = jax.random.dirichlet(jax.random.fold_in(_rk, 511), 0.3 * jnp.ones((16,), jnp.float32), (16, 1444))
        _ctx_1024t = jnp.einsum('bsk,bkd->bsd', _ctx_1024c, _ctx_1024P)
        _ctx_1024t = _ctx_1024t * jax.lax.rsqrt(jnp.mean(jnp.square(_ctx_1024t)) + 1e-12) * 0.953939
        ctx_1024 = 2.81802e-05 + 1.00001 * (_ctx_1024t + 0.3 * jax.random.normal(jax.random.fold_in(_rk, 611), (16, 1444, 128), jnp.float32))
        _validS = jnp.arange(100)[None, :] < _lenS[:, None]
        _validS2 = jnp.arange(1444)[None, :] < _lenS2[:, None]
        _causal = jnp.tril(jnp.ones((100, 100), dtype=bool))
        mask_BxS2_fk0 = jnp.where(jnp.broadcast_to(_validS2[:, :], (16, 1444)), 0.0, 1.0).astype(jnp.float32)
        _g = jax.random.normal(jax.random.fold_in(_rk, 9001), (2, 1), jnp.float32)
        _g = jnp.sign(_g) * jnp.maximum(jnp.abs(_g), 1.0) + (_g == 0) * 1.0
        g_xattn = _g[0]
        g_ffn = _g[1]
        return (x, ctx_1024, mask_BxS2_fk0, g_xattn, g_ffn)
    x, ctx_1024, mask_BxS2_fk0, g_xattn, g_ffn = _rec_inputs()

    def _L0_xattn_setup():
        import jax, jax.numpy as jnp
        import numpy as np
        B, LQ, LK, D = (8, 256, 256, 128)
        key = jax.random.key(seed)
        k1, k2, k3, k4, k5 = jax.random.split(key, 5)
        inp = jax.random.normal(k1, (B, LQ, D), dtype=jnp.float32)
        memory = jax.random.normal(k2, (B, LK, D), dtype=jnp.float32)
        mask = (jax.random.uniform(k3, (B, LK)) < 0.15).astype(jnp.float32)
        w_input = jax.random.uniform(k4, (1, D), dtype=jnp.float32, minval=-1.0 / np.sqrt(D), maxval=1.0 / np.sqrt(D))
        dot_scale = jax.random.uniform(k5, (D,), dtype=jnp.float32, minval=0.0, maxval=1.0 / np.sqrt(D))
        return {'input': inp, 'memory': memory, 'mask': mask, 'w_input': w_input, 'dot_scale': dot_scale}
    _L0_xattn_all = _L0_xattn_setup()
    _L0_xattn_in = {k: v for k, v in _L0_xattn_all.items() if k in ('w_input', 'dot_scale')}
    del _L0_xattn_all

    def _L0_ffn_setup():
        import jax, jax.numpy as jnp
        import numpy as np
        B, S, D, F, E, TOPK = (4, 256, 128, 512, 8, 2)

        def _moe_forward(x, W_router, W_gate, W_up, W_down):
            logits = jnp.einsum('bsd,ed->bse', x, W_router)
            probs = jax.nn.softmax(logits, axis=-1)
            gates, indices = jax.lax.top_k(probs, TOPK)
            gates = gates / jnp.sum(gates, axis=-1, keepdims=True)
            weights = jnp.sum(gates[..., None] * jax.nn.one_hot(indices, E, dtype=x.dtype), axis=-2)
            weights_e = jnp.moveaxis(weights, -1, 0)

            def body(acc, params):
                wg, wu, wd, wt = params
                gate = jax.nn.silu(jnp.einsum('bsd,fd->bsf', x, wg))
                up = jnp.einsum('bsd,fd->bsf', x, wu)
                y = jnp.einsum('bsf,df->bsd', gate * up, wd)
                return (acc + wt[..., None] * y, None)
            out, _ = jax.lax.scan(body, jnp.zeros_like(x), (W_gate, W_up, W_down, weights_e))
            return out
        key = jax.random.key(seed)
        k1, k2, k3, k4, k5 = jax.random.split(key, 5)
        x = jax.random.normal(k1, (B, S, D), dtype=jnp.float32)
        W_router = jax.random.normal(k2, (E, D), dtype=jnp.float32) / np.sqrt(D)
        W_gate = jax.random.normal(k3, (E, F, D), dtype=jnp.float32) / np.sqrt(D)
        W_up = jax.random.normal(k4, (E, F, D), dtype=jnp.float32) / np.sqrt(D)
        W_down = jax.random.normal(k5, (E, D, F), dtype=jnp.float32) / np.sqrt(F)
        return {'x': x, 'W_router': W_router, 'W_gate': W_gate, 'W_up': W_up, 'W_down': W_down}
    _L0_ffn_all = _L0_ffn_setup()
    _L0_ffn_in = {k: v for k, v in _L0_ffn_all.items() if k in ('W_router', 'W_gate', 'W_up', 'W_down')}
    del _L0_ffn_all
    return {'x': x, 'ctx_1024': ctx_1024, 'mask_BxS2_fk0': mask_BxS2_fk0, 'g_xattn': g_xattn, 'g_ffn': g_ffn, 'L0_xattn_w_input': _L0_xattn_in['w_input'], 'L0_xattn_dot_scale': _L0_xattn_in['dot_scale'], 'L0_ffn_W_router': _L0_ffn_in['W_router'], 'L0_ffn_W_gate': _L0_ffn_in['W_gate'], 'L0_ffn_W_up': _L0_ffn_in['W_up'], 'L0_ffn_W_down': _L0_ffn_in['W_down']}

def reference(x, ctx_1024, mask_BxS2_fk0, g_xattn, g_ffn, L0_xattn_w_input, L0_xattn_dot_scale, L0_ffn_W_router, L0_ffn_W_gate, L0_ffn_W_up, L0_ffn_W_down):
    import jax
    import jax.numpy as jnp

    def _L0_xattn_ref(input, memory, mask, w_input, dot_scale):
        import jax, jax.numpy as jnp
        import numpy as np
        B, LQ, LK, D = (8, 256, 256, 128)
        input_dot = jnp.einsum('bqd,od->bqo', input, w_input)
        cross_dot = jnp.einsum('bqd,bkd->bqk', input * dot_scale, memory)
        att = input_dot + cross_dot - 1e+30 * mask[:, None, :]
        weight_one = jax.nn.softmax(att, axis=-1)
        output_one = jnp.einsum('bqk,bkd->bqd', weight_one, memory)
        return output_one

    def _L0_ffn_ref(x, W_router, W_gate, W_up, W_down):
        import jax, jax.numpy as jnp
        import numpy as np
        B, S, D, F, E, TOPK = (4, 256, 128, 512, 8, 2)

        def _moe_forward(x, W_router, W_gate, W_up, W_down):
            logits = jnp.einsum('bsd,ed->bse', x, W_router)
            probs = jax.nn.softmax(logits, axis=-1)
            gates, indices = jax.lax.top_k(probs, TOPK)
            gates = gates / jnp.sum(gates, axis=-1, keepdims=True)
            weights = jnp.sum(gates[..., None] * jax.nn.one_hot(indices, E, dtype=x.dtype), axis=-2)
            weights_e = jnp.moveaxis(weights, -1, 0)

            def body(acc, params):
                wg, wu, wd, wt = params
                gate = jax.nn.silu(jnp.einsum('bsd,fd->bsf', x, wg))
                up = jnp.einsum('bsd,fd->bsf', x, wu)
                y = jnp.einsum('bsf,df->bsd', gate * up, wd)
                return (acc + wt[..., None] * y, None)
            out, _ = jax.lax.scan(body, jnp.zeros_like(x), (W_gate, W_up, W_down, weights_e))
            return out
        return _moe_forward(x, W_router, W_gate, W_up, W_down)
    x = x + jnp.tanh(g_xattn[0]) * _L0_xattn_ref(_layernorm(x, axis=-1), ctx_1024, mask_BxS2_fk0, L0_xattn_w_input, L0_xattn_dot_scale)
    x = x + jnp.tanh(g_ffn[0]) * _L0_ffn_ref(_layernorm(x, axis=-1), L0_ffn_W_router, L0_ffn_W_gate, L0_ffn_W_up, L0_ffn_W_down)
    return x

_drawn_inputs = setup_inputs


def setup_inputs(seed=0):
    import zlib

    import numpy as np

    out = dict(_drawn_inputs(seed))
    spreads = {}
    factors = {}
    for name, (base, spread) in spreads.items():
        noise = np.random.default_rng([zlib.crc32(name.encode()), seed]).standard_normal(out[name].shape)
        drawn = base * np.exp(spread * noise) if base else spread * noise
        out[name] = jnp.asarray(drawn.astype(out[name].dtype))
    for name, factor in factors.items():
        out[name] = (out[name] * factor).astype(out[name].dtype)
    return out
```

```python
from contextlib import ExitStack

import concourse.bass as bass
from concourse import mybir

ALU = mybir.AluOpType
ACT = mybir.ActivationFunctionType
F32 = mybir.dt.float32
I32 = mybir.dt.int32
X = mybir.AxisListType.X

P = 128
CHUNKS = 12
GROUPS = 3
GROUP = CHUNKS // GROUPS
RING = 4
NEG = -1e30
LOWEST = -3.0e38
EPS = 1e-5


def key_order(keys):
    full, extra = divmod(keys, CHUNKS)
    rows = [full + (c < extra) for c in range(CHUNKS)]
    starts = [sum(rows[:c]) for c in range(CHUNKS)]
    return rows, starts


def build(nc, x, ctx, mask, g_xattn, g_ffn, w_input, dot_scale, w_router, w_gate, w_up, w_down, out):
    B, Q, D = x.shape
    K = ctx.shape[1]
    E = w_router.shape[1]
    F = w_gate.shape[2]
    FC = F // P
    rows, starts = key_order(K)
    full = K // CHUNKS
    extra = K - full * CHUNKS
    group_start = [starts[g * GROUP] for g in range(GROUPS)] + [K]
    assert D == P and Q + GROUP * Q <= 512 and B % RING == 0

    mask_scaled = nc.dram_tensor("mask_scaled", [B, K], F32).ap()

    with ExitStack() as stack:
        def sb(name, shape, dt=F32):
            return stack.enter_context(nc.sbuf_tensor(name, shape, dt))

        def sem(name):
            return stack.enter_context(nc.semaphore(name))

        psum = stack.enter_context(nc.psum_tensor("psum", [P, 8, 512], F32))
        scores_ps = psum[:, 0:3, :].rearrange("p a n -> p (a n)")
        ctxT_ps = [psum[:, 3, :], psum[:, 4, :]]
        probsT_ps = [psum[:, 5, :], psum[:, 6, :]]
        attn_ps = psum[:, 7, 0:D]

        identity = sb("identity", [P, P])
        x_all = sb("x_all", [Q, B, D])
        x2_all = sb("x2_all", [Q, B, D])
        mask_rows = sb("mask_rows", [B, K])
        mask_neg = sb("mask_neg", [B, K])
        maskb = sb("maskb", [Q, 2, K])
        wi_col = sb("wi_col", [P, 1])
        ds_col = sb("ds_col", [P, 1])
        gates_in = sb("gates_in", [P, 2])
        tanh_g = sb("tanh_g", [P, 2])
        wr_sb = sb("wr_sb", [P, E])
        wg_sb = sb("wg_sb", [P, E, F])
        wu_sb = sb("wu_sb", [P, E, F])
        wd_sb = sb("wd_sb", [P, E, FC, D])
        ctx_sb = [sb(f"ctx_sb{s}", [full + 1, CHUNKS, D]) for s in range(RING)]
        ctxT = sb("ctxT", [P, K])
        stats1 = sb("stats1", [Q, 6])
        mv1 = sb("mv1", [Q, 2])
        rstd1 = sb("rstd1", [Q, 1])
        var1 = sb("var1", [Q, 1])
        var2 = sb("var2", [Q, 1])
        power = sb("power", [Q, 1])
        xn = sb("xn", [Q, 2, D])
        qT = sb("qT", [P, 2, Q])
        scores = sb("scores", [Q, 2, K])
        probs = sb("probs", [Q, 2, K])
        probsT = sb("probsT", [P, CHUNKS, Q])
        rowmax = sb("rowmax", [Q, 2])
        negmax = sb("negmax", [Q, 2])
        rowsum = sb("rowsum", [Q, 2])
        recip = sb("recip", [Q, 2])
        gain = sb("gain", [Q, 2])

        stats2 = sb("stats2", [Q, 6])
        mv2 = sb("mv2", [Q, 2])
        rstd2 = sb("rstd2", [Q, 1])
        xn2 = sb("xn2", [Q, 2, D])
        xT2 = sb("xT2", [P, 2, Q])
        logits = sb("logits", [Q, B, E])
        expert_i = sb("expert_i", [Q, B, E], I32)
        expert_m8 = sb("expert_m8", [Q, B, E])
        eq = sb("eq", [Q, B, E])
        first = sb("first", [Q, B, E])
        second = sb("second", [Q, B, E])
        rest = sb("rest", [Q, B, E])
        weights = sb("weights", [Q, B, E])
        m1 = sb("m1", [Q, B])
        m2 = sb("m2", [Q, B])
        idx = sb("idx", [Q, B])
        t2 = sb("t2", [Q, B])
        t1 = sb("t1", [Q, B])
        den = sb("den", [Q, B])
        gate1 = sb("gate1", [Q, B])
        gate2 = sb("gate2", [Q, B])
        xT_all = sb("xT_all", [P, B, Q])
        xT_e = sb("xT_e", [P, 2, Q])
        sil = sb("sil", [Q, 2, F])
        hid = sb("hid", [Q, 2, F])
        hidT = sb("hidT", [P, 2, FC, Q])
        out_sb = sb("out_sb", [Q, 2, D])

        x_first = sem("x_first")
        x_rest = sem("x_rest")
        small_loaded = sem("small_loaded")
        mask_raw = sem("mask_raw")
        mask_scaled_done = sem("mask_scaled_done")
        mask_stored = sem("mask_stored")
        mask_loaded = [sem(f"mask_loaded{s}") for s in range(2)]
        ctx_loaded = [sem(f"ctx_loaded{s}") for s in range(RING)]
        weights_loaded = sem("weights_loaded")
        identity_zeroed = sem("identity_zeroed")
        identity_done = sem("identity_done")
        var1_done = sem("var1_done")
        var2_done = sem("var2_done")
        power_set = sem("power_set")
        tanh_done = sem("tanh_done")
        stats1_done = sem("stats1_done")
        mv1_done = sem("mv1_done")
        rstd1_done = sem("rstd1_done")
        xn_done = sem("xn_done")
        qT_raw = sem("qT_raw")
        qT_done = sem("qT_done")
        ctxT_raw = sem("ctxT_raw")
        ctxT_act = sem("ctxT_act")
        ctxT_dve = sem("ctxT_dve")
        scores_raw = sem("scores_raw")
        scores_done = sem("scores_done")
        negmax_done = sem("negmax_done")
        probs_done = sem("probs_done")
        probsT_raw = sem("probsT_raw")
        probsT_done = sem("probsT_done")
        attn_raw = sem("attn_raw")
        recip_done = sem("recip_done")
        gain_done = sem("gain_done")
        x2_done = sem("x2_done")

        stats2_done = sem("stats2_done")
        mv2_done = sem("mv2_done")
        rstd2_done = sem("rstd2_done")
        xn2_done = sem("xn2_done")
        xT2_raw = sem("xT2_raw")
        xT2_done = sem("xT2_done")
        logits_raw = sem("logits_raw")
        logits_done = sem("logits_done")
        iota_done = sem("iota_done")
        route_step = sem("route_step")
        t2_done = sem("t2_done")
        xTe_done = sem("xTe_done")
        gu_done = sem("gu_done")
        sil_done = sem("sil_done")
        hid_done = sem("hid_done")
        hidT_raw = sem("hidT_raw")
        hidT_done = sem("hidT_done")
        y_done = sem("y_done")
        out_done = sem("out_done")
        out_stored = sem("out_stored")

        def wait(eng, semaphore, value):
            if not isinstance(value, int) or value > 0:
                eng.wait_ge(semaphore, value)

        def over_batches(eng, step):
            step(0, 0)
            step(0, 1)
            with eng.Fori(0, (B - RING) // RING) as i:
                for k in range(2, RING + 2):
                    step(i, k)
            for k in range(B - RING + 2, B):
                step(0, k)

        def apart(eng):
            eng.nop(nofuse=True)

        block = stack.enter_context(nc.Block())

        @block.sync
        def _(sp):
            def load_ctx(b, slot):
                sp.dma_start(ctx_sb[slot][0:full, :, :],
                             ctx[b, 0:full * CHUNKS, :].rearrange("(p c) d -> p c d", c=CHUNKS)).then_inc(ctx_loaded[slot], 16)
                sp.dma_start(ctx_sb[slot][full:full + 1, 0:extra, :],
                             ctx[b, full * CHUNKS:K, :].rearrange("(p c) d -> p c d", p=1)).then_inc(ctx_loaded[slot], 16)

            def load_mask(b, slot):
                sp.dma_start(maskb[:, slot, :], mask_scaled[b, :].partition_broadcast(Q)).then_inc(mask_loaded[slot], 16)

            sp.dma_start(mask_rows[:, :], mask).then_inc(mask_raw, 16)
            sp.dma_start(x_all[:, 0:1, :], x[0:1, :, :].rearrange("b q d -> q b d")).then_inc(x_first, 16)
            load_ctx(0, 0)
            sp.dma_start(x_all[:, 1:B, :], x[1:B, :, :].rearrange("b q d -> q b d")).then_inc(x_rest, 16)
            load_ctx(1, 1)
            sp.wait_ge(mask_scaled_done, 1)
            sp.dma_start(mask_scaled, mask_neg[:, :]).then_inc(mask_stored, 16)
            sp.wait_ge(mask_stored, 16)
            load_mask(0, 0)
            load_mask(1, 1)
            load_ctx(2, 2)
            load_ctx(3, 3)
            with sp.Fori(0, (B - RING) // RING) as i:
                for k in range(RING):
                    sp.wait_ge(scores_done, i * RING + k + 1)
                    load_mask(i * RING + (k + 2), k % 2)
                    sp.wait_ge(attn_raw, i * RING + k + 1)
                    load_ctx(i * RING + (k + RING), k)
            for k in range(B - RING, B - 2):
                sp.wait_ge(scores_done, k + 1)
                load_mask(k + 2, k % 2)

            for b in range(B):
                sp.wait_ge(out_done, b + 1)
                sp.dma_start(out[b, :, :], out_sb[:, b % 2, :]).then_inc(out_stored, 16)
            sp.wait_ge(out_stored, 16 * B)

        @block.gpsimd
        def _(pool):
            nc.gpsimd.memset(identity[:, :], 0.0).then_inc(identity_zeroed, 1)
            pool.wait_ge(identity_zeroed, 1)
            nc.gpsimd.affine_select(out=identity[:, :], in_=identity[:, :], compare_op=ALU.not_equal, fill=1.0,
                                    base=0, pattern=[[-1, P]], channel_multiplier=1).then_inc(identity_done, 1)
            nc.gpsimd.iota(expert_i[:, :, :], pattern=[[0, B], [1, E]], base=-E, channel_multiplier=0).then_inc(iota_done, 1)
            nc.gpsimd.memset(power[:, :], -0.5).then_inc(power_set, 1)
            pool.wait_ge(power_set, 1)
            for mv, var, rstd, mv_done, var_done, rstd_done in ((mv1, var1, rstd1, mv1_done, var1_done, rstd1_done),
                                                                (mv2, var2, rstd2, mv2_done, var2_done, rstd2_done)):
                with pool.Fori(0, B) as b:
                    pool.wait_ge(mv_done, b + 1)
                    apart(pool)
                    nc.gpsimd.tensor_scalar(var[:, :], mv[:, 1:2], EPS, None, ALU.add).then_inc(var_done, 1)
                    pool.wait_ge(var_done, b + 1)
                    nc.gpsimd.tensor_tensor(rstd[:, :], var[:, :], power[:, :], ALU.pow).then_inc(rstd_done, 1)

        @block.scalar
        def _(act):
            act.dma_start(wi_col[:, :], w_input.rearrange("o d -> d o")).then_inc(small_loaded, 16)
            act.dma_start(ds_col[:, :], dot_scale.rearrange("(d o) -> d o", o=1)).then_inc(small_loaded, 16)
            act.dma_start(gates_in[:, 0:1], g_xattn.partition_broadcast(P)).then_inc(small_loaded, 16)
            act.dma_start(gates_in[:, 1:2], g_ffn.partition_broadcast(P)).then_inc(small_loaded, 16)
            act.dma_start(wr_sb[:, :], w_router).then_inc(weights_loaded, 16)
            act.dma_start(wg_sb[:, :, :], w_gate).then_inc(weights_loaded, 16)
            act.dma_start(wu_sb[:, :, :], w_up).then_inc(weights_loaded, 16)
            act.dma_start(wd_sb[:, :, :, :], w_down).then_inc(weights_loaded, 16)
            act.wait_ge(small_loaded, 64)
            nc.scalar.activation(tanh_g[:, :], gates_in[:, :], ACT.Tanh).then_inc(tanh_done, 1)

            def evacuate_ctxT(i, k):
                b = i * RING + k
                act.wait_ge(ctxT_raw, b * GROUPS + 1)
                wait(act, scores_raw, b)
                nc.scalar.activation(ctxT[:, 0:group_start[1]], ctxT_ps[(k * GROUPS) % 2][:, 0:group_start[1]],
                                     ACT.Identity, bias=wi_col[:, 0:1], scale=ds_col[:, 0:1]).then_inc(ctxT_act, 1)

            def evacuate_qT(i, k):
                b = i * RING + k
                act.wait_ge(qT_raw, b + 1)
                nc.scalar.activation(qT[:, k % 2, :], probsT_ps[((k - 2) * GROUPS) % 2][:, GROUP * Q:GROUP * Q + Q],
                                     ACT.Copy).then_inc(qT_done, 1)

            def evacuate_probsT(i, k, g):
                b = i * RING + k
                act.wait_ge(probsT_raw, b * GROUPS + g + 1)
                wait(act, attn_raw, b)
                n = rows[g * GROUP]
                nc.scalar.activation(probsT[0:n, g * GROUP:(g + 1) * GROUP, :],
                                     probsT_ps[(k * GROUPS + g) % 2][0:n, 0:GROUP * Q].rearrange("p (c q) -> p c q", c=GROUP),
                                     ACT.Copy).then_inc(probsT_done, 1)

            def step(i, k):
                b = i * RING + k
                if k > 0:
                    for g in range(GROUPS):
                        if g == 0 and k + 1 < B:
                            act.wait_ge(probsT_raw, (b - 1) * GROUPS + 1)
                            evacuate_qT(i, k + 1)
                        evacuate_probsT(i, k - 1, g)
                elif k + 1 < B:
                    evacuate_qT(i, k + 1)
                if k + 1 < B:
                    evacuate_ctxT(i, k + 1)
                act.wait_ge(negmax_done, b + 1)
                wait(act, probsT_raw, (b - 1) * GROUPS)
                nc.scalar.activation(probs[:, k % 2, :], scores[:, k % 2, :], ACT.Exp, bias=negmax[:, k % 2:k % 2 + 1],
                                     accum_out=rowsum[:, k % 2:k % 2 + 1]).then_inc(probs_done, 1)

            evacuate_qT(0, 0)
            evacuate_ctxT(0, 0)
            over_batches(act, step)
            for g in range(GROUPS):
                evacuate_probsT(0, B - 1, g)

            def section1(i):
                for k in range(2):
                    b = i * 2 + k
                    act.wait_ge(xT2_raw, b + 1)
                    nc.scalar.activation(xT2[:, k, :], ctxT_ps[k][:, 0:Q], ACT.Copy).then_inc(xT2_done, 1)

            section1(0)
            with act.Fori(1, B // 2) as i:
                section1(i)

            act.wait_ge(route_step, 10)
            nc.scalar.activation(t2[:, :], t1[:, :], ACT.Exp).then_inc(t2_done, 1)

            def section2(i):
                for e in range(E + 1):
                    n = i * E + e
                    if e < E:
                        act.wait_ge(gu_done, n + 1)
                        wait(act, hid_done, n - 1 if e > 0 else n)
                        nc.scalar.activation(sil[:, e % 2, :], psum[0:Q, e % 2, :], ACT.Silu).then_inc(sil_done, 1)
                    if e > 0:
                        act.wait_ge(hidT_raw, n)
                        nc.scalar.activation(hidT[:, (e - 1) % 2, :, :], psum[:, 4 + (e - 1) % 2, 0:FC * Q].rearrange(
                            "p (c q) -> p c q", c=FC), ACT.Copy).then_inc(hidT_done, 1)

            section2(0)
            with act.Fori(1, B) as i:
                section2(i)

        @block.vector
        def _(dve):
            dve.wait_ge(mask_raw, 16)
            nc.vector.tensor_scalar(mask_neg[:, :], mask_rows[:, :], NEG, None, ALU.mult).then_inc(mask_scaled_done, 1)
            dve.wait_ge(small_loaded, 64)
            dve.wait_ge(tanh_done, 1)

            def layer_norm(i, k):
                b = i * RING + k
                dve.wait_ge(x_first if k == 0 else x_rest, 16)
                wait(dve, mv1_done, b)
                nc.vector.bn_stats(stats1[:, :], x_all[:, b, :]).then_inc(stats1_done, 1)
                dve.wait_ge(stats1_done, b + 1)
                wait(dve, xn_done, b)
                apart(dve)
                nc.vector.bn_aggr(mv1[:, :], stats1[:, :]).then_inc(mv1_done, 1)
                dve.wait_ge(mv1_done, b + 1)
                dve.wait_ge(rstd1_done, b + 1)
                wait(dve, qT_raw, b - 1)
                nc.vector.tensor_scalar(xn[:, k % 2, :], x_all[:, b, :], mv1[:, 0:1], rstd1[:, 0:1],
                                        ALU.subtract, ALU.mult).then_inc(xn_done, 1)

            def evacuate_ctxT(i, k, g):
                b = i * RING + k
                dve.wait_ge(ctxT_raw, b * GROUPS + g + 1)
                n = group_start[g + 1] - group_start[g]
                nc.vector.tensor_scalar(ctxT[:, group_start[g]:group_start[g + 1]], ctxT_ps[(k * GROUPS + g) % 2][:, 0:n],
                                        ds_col[:, 0:1], wi_col[:, 0:1], ALU.mult, ALU.add).then_inc(ctxT_dve, 1)

            def residual(i, k):
                b = i * RING + k
                s = slice(k % 2, k % 2 + 1)
                dve.wait_ge(probs_done, b + 1)
                nc.vector.reciprocal(recip[:, s], rowsum[:, s]).then_inc(recip_done, 1)
                dve.wait_ge(recip_done, b + 1)
                nc.vector.tensor_scalar(gain[:, s], recip[:, s], tanh_g[0:Q, 0:1], None, ALU.mult).then_inc(gain_done, 1)
                dve.wait_ge(gain_done, b + 1)
                dve.wait_ge(attn_raw, b + 1)
                nc.vector.scalar_tensor_tensor(out=x2_all[:, b, :], in0=attn_ps[0:Q, :], scalar=gain[:, s], in1=x_all[:, b, :],
                                               op0=ALU.mult, op1=ALU.add).then_inc(x2_done, 1)

            def step(i, k):
                b = i * RING + k
                if k + 1 < B:
                    layer_norm(i, k + 1)
                s = slice(k % 2, k % 2 + 1)
                dve.wait_ge(scores_raw, b + 1)
                dve.wait_ge(mask_loaded[k % 2], i * (16 * RING // 2) + 16 * (k // 2 + 1))
                wait(dve, probs_done, b - 1)
                apart(dve)
                nc.vector.tensor_tensor_reduce(out=scores[:, k % 2, :], in0=scores_ps[0:Q, 0:K], in1=maskb[:, k % 2, :],
                                               scale=1.0, scalar=LOWEST, op0=ALU.add, op1=ALU.max,
                                               accum_out=rowmax[:, s]).then_inc(scores_done, 1)
                dve.wait_ge(scores_done, b + 1)
                nc.vector.tensor_scalar(negmax[:, s], rowmax[:, s], -1.0, None, ALU.mult).then_inc(negmax_done, 1)
                if k + 1 < B:
                    evacuate_ctxT(i, k + 1, 1)
                    evacuate_ctxT(i, k + 1, 2)
                if k > 0:
                    residual(i, k - 1)

            layer_norm(0, 0)
            evacuate_ctxT(0, 0, 1)
            evacuate_ctxT(0, 0, 2)
            over_batches(dve, step)
            residual(0, B - 1)

            def norm2(i, k, n):
                b = i * 2 + k
                dve.wait_ge(x2_done, b + 1)
                nc.vector.bn_stats(stats2[:, :], x2_all[:, b, :]).then_inc(stats2_done, 1)
                dve.wait_ge(stats2_done, b + 1)
                apart(dve)
                nc.vector.bn_aggr(mv2[:, :], stats2[:, :]).then_inc(mv2_done, 1)
                dve.wait_ge(mv2_done, b + 1)
                dve.wait_ge(rstd2_done, b + 1)
                nc.vector.tensor_scalar(xn2[:, k, :], x2_all[:, b, :], mv2[:, 0:1], rstd2[:, 0:1],
                                        ALU.subtract, ALU.mult).then_inc(xn2_done, 1)
                dve.wait_ge(xn2_done, b + 1)
                dve.wait_ge(logits_raw, b + 1)
                nc.vector.tensor_copy(logits[:, b, :], probsT_ps[k][0:Q, 0:E]).then_inc(logits_done, 1)
                nc.vector.tensor_copy(xT_all[:, b, :], xT2[:, k, :]).then_inc(logits_done, 1)

            def section3(i):
                for k in range(2):
                    norm2(i, k, 0)

            section3(0)
            with dve.Fori(1, B // 2) as i:
                section3(i)

            steps = [0]

            def link(ins):
                steps[0] += 1
                ins.then_inc(route_step, 1)
                dve.wait_ge(route_step, steps[0])

            def wide(a):
                return a[:, :].unsqueeze(2).to_broadcast([Q, B, E])

            dve.wait_ge(logits_done, 2 * B)
            dve.wait_ge(iota_done, 1)
            link(nc.vector.tensor_copy(expert_m8[:, :, :], expert_i[:, :, :]))
            link(nc.vector.tensor_reduce(m1[:, :], logits[:, :, :], axis=X, op=ALU.max))
            link(nc.vector.tensor_tensor(eq[:, :, :], logits[:, :, :], wide(m1), ALU.is_equal))
            link(nc.vector.tensor_tensor(eq[:, :, :], eq[:, :, :], expert_m8[:, :, :], ALU.mult))
            link(nc.vector.tensor_reduce(idx[:, :], eq[:, :, :], axis=X, op=ALU.min))
            link(nc.vector.tensor_tensor(first[:, :, :], expert_m8[:, :, :], wide(idx), ALU.is_equal))
            link(nc.vector.scalar_tensor_tensor(out=rest[:, :, :], in0=first[:, :, :], scalar=LOWEST, in1=logits[:, :, :],
                                                op0=ALU.mult, op1=ALU.add))
            link(nc.vector.tensor_reduce(m2[:, :], rest[:, :, :], axis=X, op=ALU.max))
            link(nc.vector.tensor_tensor(eq[:, :, :], rest[:, :, :], wide(m2), ALU.is_equal))
            link(nc.vector.tensor_tensor(t1[:, :], m2[:, :], m1[:, :], ALU.subtract))
            link(nc.vector.tensor_tensor(eq[:, :, :], eq[:, :, :], expert_m8[:, :, :], ALU.mult))
            link(nc.vector.tensor_reduce(idx[:, :], eq[:, :, :], axis=X, op=ALU.min))
            link(nc.vector.tensor_tensor(second[:, :, :], expert_m8[:, :, :], wide(idx), ALU.is_equal))
            dve.wait_ge(t2_done, 1)
            link(nc.vector.tensor_scalar(den[:, :], t2[:, :], 1.0, None, ALU.add))
            link(nc.vector.reciprocal(gate1[:, :], den[:, :]))
            link(nc.vector.tensor_tensor(gate2[:, :], gate1[:, :], t2[:, :], ALU.mult))
            link(nc.vector.tensor_tensor(first[:, :, :], first[:, :, :], wide(gate1), ALU.mult))
            link(nc.vector.tensor_tensor(second[:, :, :], second[:, :, :], wide(gate2), ALU.mult))
            link(nc.vector.tensor_tensor(weights[:, :, :], first[:, :, :], second[:, :, :], ALU.add))

            def section4(i):
                for k in range(2):
                    b = i * 2 + k
                    wait(dve, y_done, b)
                    nc.vector.tensor_copy(xT_e[:, k, :], xT_all[:, b, :]).then_inc(xTe_done, 1)
                    for e in range(E):
                        n = b * E + e
                        dve.wait_ge(sil_done, n + 1)
                        wait(dve, hidT_raw, n - 1 if e > 0 else n)
                        nc.vector.scalar_tensor_tensor(
                            out=hid[:, e % 2, :], in0=sil[:, e % 2, :], scalar=weights[:, b, e:e + 1],
                            in1=psum[0:Q, 2 + e % 2, :], op0=ALU.mult, op1=ALU.mult).then_inc(hid_done, 1)
                    dve.wait_ge(y_done, b + 1)
                    wait(dve, out_stored, b * 16)
                    nc.vector.scalar_tensor_tensor(out=out_sb[:, k, :], in0=psum[0:Q, 6, 0:D], scalar=tanh_g[0:Q, 1:2],
                                                   in1=x2_all[:, b, :], op0=ALU.mult, op1=ALU.add).then_inc(out_done, 1)

            section4(0)
            with dve.Fori(1, B // 2) as i:
                section4(i)

        @block.tensor
        def _(pe):
            pe.wait_ge(identity_done, 1)

            def transpose_q(i, k):
                b = i * RING + k
                pe.wait_ge(xn_done, b + 1)
                nc.tensor.transpose(probsT_ps[((k - 2) * GROUPS) % 2][:, GROUP * Q:GROUP * Q + Q], xn[:, k % 2, :],
                                    identity[0:Q, 0:Q]).then_inc(qT_raw, 1)

            def transpose_ctx(i, k):
                b = i * RING + k
                slot = k % RING
                pe.wait_ge(ctx_loaded[slot], i * 32 + 32 * (k // RING + 1))
                for g in range(GROUPS):
                    if g == 2:
                        pe.wait_ge(ctxT_act, b + 1)
                    else:
                        wait(pe, ctxT_dve, 2 * b - 1 + g)
                    for c in range(g * GROUP, (g + 1) * GROUP):
                        at = starts[c] - group_start[g]
                        last = nc.tensor.transpose(ctxT_ps[(k * GROUPS + g) % 2][:, at:at + rows[c]],
                                                   ctx_sb[slot][0:rows[c], c, :], identity[0:rows[c], 0:rows[c]])
                    last.then_inc(ctxT_raw, 1)

            def score(i, k):
                b = i * RING + k
                pe.wait_ge(qT_done, b + 1)
                pe.wait_ge(ctxT_act, b + 1)
                pe.wait_ge(ctxT_dve, 2 * b + 2)
                wait(pe, scores_done, b)
                for n in range(0, K, 512):
                    m = min(512, K - n)
                    last = nc.tensor.matmul(scores_ps[0:Q, n:n + m], qT[:, k % 2, :], ctxT[:, n:n + m], start=True, stop=True)
                last.then_inc(scores_raw, 1)

            def transpose_probs(i, k, q_too):
                b = i * RING + k
                pe.wait_ge(probs_done, b + 1)
                for g in range(GROUPS):
                    wait(pe, probsT_done, b * GROUPS + g - 1)
                    if g == 0 and q_too:
                        transpose_q(i, k + 2)
                    for c in range(g * GROUP, (g + 1) * GROUP):
                        at = (c - g * GROUP) * Q
                        last = nc.tensor.transpose(probsT_ps[(k * GROUPS + g) % 2][0:rows[c], at:at + Q],
                                                   probs[:, k % 2, starts[c]:starts[c] + rows[c]], identity[0:Q, 0:Q])
                    last.then_inc(probsT_raw, 1)

            def attend(i, k):
                b = i * RING + k
                wait(pe, x2_done, b)
                for g in range(GROUPS):
                    pe.wait_ge(probsT_done, b * GROUPS + g + 1)
                    for c in range(g * GROUP, (g + 1) * GROUP):
                        last = nc.tensor.matmul(attn_ps[0:Q, :], probsT[0:rows[c], c, :], ctx_sb[k % RING][0:rows[c], c, :],
                                                start=(c == 0), stop=(c == CHUNKS - 1))
                last.then_inc(attn_raw, 1)

            def step(i, k):
                score(i, k)
                if k > 0:
                    transpose_probs(i, k - 1, k + 1 < B)
                elif k + 1 < B:
                    transpose_q(i, k + 1)
                if k + 1 < B:
                    transpose_ctx(i, k + 1)
                if k > 0:
                    attend(i, k - 1)

            transpose_q(0, 0)
            transpose_ctx(0, 0)
            over_batches(pe, step)
            transpose_probs(0, B - 1, False)
            attend(0, B - 1)

            pe.wait_ge(weights_loaded, 64)
            pe.wait_ge(x2_done, B)
            def section5(i):
                for k in range(2):
                    b = i * 2 + k
                    pe.wait_ge(xn2_done, b + 1)
                    nc.tensor.transpose(ctxT_ps[k][:, 0:Q], xn2[:, k, :], identity[0:Q, 0:Q]).then_inc(xT2_raw, 1)
                    pe.wait_ge(xT2_done, b + 1)
                    nc.tensor.matmul(probsT_ps[k][0:Q, 0:E], xT2[:, k, :], wr_sb[:, :], start=True, stop=True).then_inc(logits_raw, 1)

            section5(0)
            with pe.Fori(1, B // 2) as i:
                section5(i)

            pe.wait_ge(route_step, 19)

            def gate_up(b, k, e, n):
                wait(pe, hid_done, n - 1 if e > 0 else n)
                nc.tensor.matmul(psum[0:Q, e % 2, :], xT_e[:, k, :], wg_sb[:, e, :], start=True, stop=True)
                nc.tensor.matmul(psum[0:Q, 2 + e % 2, :], xT_e[:, k, :], wu_sb[:, e, :], start=True, stop=True).then_inc(gu_done, 1)

            def down(b, e, n):
                pe.wait_ge(hid_done, n + 1)
                for c in range(FC):
                    last = nc.tensor.transpose(psum[:, 4 + e % 2, c * Q:(c + 1) * Q], hid[:, e % 2, c * P:(c + 1) * P], identity[0:Q, 0:Q])
                last.then_inc(hidT_raw, 1)
                pe.wait_ge(hidT_done, n + 1)
                if e == 0:
                    wait(pe, out_done, b)
                for c in range(FC):
                    last = nc.tensor.matmul(psum[0:Q, 6, 0:D], hidT[:, e % 2, c, :], wd_sb[:, e, c, :],
                                            start=(e == 0 and c == 0), stop=(e == E - 1 and c == FC - 1))
                if e == E - 1:
                    last.then_inc(y_done, 1)

            def section6(i):
                for k in range(2):
                    b = i * 2 + k
                    pe.wait_ge(xTe_done, b + 1)
                    for e in range(E + 1):
                        if e < E:
                            gate_up(b, k, e, b * E + e)
                        if e > 0:
                            down(b, e - 1, b * E + e - 1)

            section6(0)
            with pe.Fori(1, B // 2) as i:
                section6(i)

_IN = ["x", "ctx", "mask", "g_xattn", "g_ffn", "w_input", "dot_scale", "w_router", "w_gate", "w_up", "w_down"]


def kernel(**inputs):
    import numpy as np
    import concourse.bacc as bacc
    from concourse.bass_utils import run_bass_kernel_spmd

    a = {k: np.asarray(v) for k, v in inputs.items()}
    mask = a["mask_BxS2_fk0"]
    K = mask.shape[1]
    rows, _ = key_order(K)
    order = np.concatenate([np.arange(rows[c]) * CHUNKS + c for c in range(CHUNKS)])
    E, F, D = a["L0_ffn_W_gate"].shape
    laid = {
        "x": a["x"],
        "ctx": a["ctx_1024"],
        "mask": mask[:, order],
        "g_xattn": a["g_xattn"],
        "g_ffn": a["g_ffn"],
        "w_input": a["L0_xattn_w_input"],
        "dot_scale": a["L0_xattn_dot_scale"],
        "w_router": a["L0_ffn_W_router"].T,
        "w_gate": a["L0_ffn_W_gate"].transpose(2, 0, 1),
        "w_up": a["L0_ffn_W_up"].transpose(2, 0, 1),
        "w_down": a["L0_ffn_W_down"].reshape(E, D, F // P, P).transpose(3, 0, 2, 1),
    }
    nc = bacc.Bacc("TRN2", target_bir_lowering=False, num_devices=1)
    arrays, args = {}, []
    for name in _IN:
        v = np.ascontiguousarray(laid[name])
        arrays[f"in_{name}"] = v
        args.append(nc.dram_tensor(f"in_{name}", v.shape, mybir.dt.from_np(v.dtype), kind="ExternalInput").ap())
    out = nc.dram_tensor("out_0", a["x"].shape, F32, kind="ExternalOutput").ap()
    build(nc, *args, out)
    r = run_bass_kernel_spmd(nc, [arrays], core_ids=[0])
    return r.results[0]["out_0"]
```

```python
from contextlib import ExitStack

import concourse.bass as bass
from concourse import mybir

ALU = mybir.AluOpType
ACT = mybir.ActivationFunctionType
F32 = mybir.dt.float32
F32R = mybir.dt.float32r
I32 = mybir.dt.int32
U32 = mybir.dt.uint32
X = mybir.AxisListType.X

P = 128
CHUNKS = 12
GROUPS = 3
GROUP = CHUNKS // GROUPS
RING = 4
LAG = 3
NEG = -1e30
LOWEST = -3.0e38
EPS = 1e-5
EULER = 2.718281828459045


def key_order(keys):
    full, extra = divmod(keys, CHUNKS)
    rows = [full + (c < extra) for c in range(CHUNKS)]
    starts = [sum(rows[:c]) for c in range(CHUNKS)]
    return rows, starts


def build(nc, x, ctx, mask, g_xattn, g_ffn, w_input, dot_scale, w_router, w_experts, out):
    B, Q, D = x.shape
    K = ctx.shape[1]
    E = w_router.shape[1]
    W = w_experts.shape[1]
    F = W // 3 // E
    FC = F // P
    WC = W // B
    UP, DOWN = E * F, 2 * E * F
    rows, starts = key_order(K)
    full = K // CHUNKS
    extra = K - full * CHUNKS
    group_start = [starts[g * GROUP] for g in range(GROUPS)] + [K]
    assert D == P and (GROUP + 1) * Q <= 512 and B % RING == 0 and F == 512

    PARTS = [(0, B // 2), (B // 2, B)]
    TILES = [(2 * Q * (b1 - b0) - E) // P + E for b0, b1 in PARTS]
    T = sum(TILES)
    SLOT0 = [0, TILES[0] * P]
    PAIRS = 2 * B * Q
    ROW = D + 2
    assert T % RING == 0 and TILES[0] % RING == 0

    mask_scaled = nc.dram_tensor("mask_scaled", [B, K], F32).ap()
    slots = nc.dram_tensor("slots", [T * P, ROW], F32).ap()
    results = nc.dram_tensor("results", [PAIRS + RING * P, D], F32).ap()

    with ExitStack() as stack:
        def sb(name, shape, dt=F32):
            return stack.enter_context(nc.sbuf_tensor(name, shape, dt))

        def sem(name):
            return stack.enter_context(nc.semaphore(name))

        psum = stack.enter_context(nc.psum_tensor("psum", [P, 8, 512], F32))
        scores_ps = psum[:, 0:3, :].rearrange("p a n -> p (a n)")
        ring_ps = [psum[:, 3 + g, :] for g in range(GROUPS)]
        router_ps = psum[:, 6, :]
        attn_ps = psum[:, 7, :]
        gate_ps = [psum[:, 0, :], psum[:, 2, :]]
        up_ps = [psum[:, 1, :], psum[:, 3, :]]
        hidT_ps = psum[:, 4, :]
        rowT_ps = psum[:, 5, 0:P]
        y_ps = psum[:, 7, 0:D]

        identity = sb("identity", [P, P])
        x_all = sb("x_all", [Q, B, D])
        maskb = sb("maskb", [Q, 2, K])
        wi_col = sb("wi_col", [P, 1])
        ds_col = sb("ds_col", [P, 1])
        gates_in = sb("gates_in", [P, 2])
        tanh_g = sb("tanh_g", [P, 2])
        wr_sb = sb("wr_sb", [P, E])
        w_raw = sb("w_raw", [P, 2, WC])
        w_hi = sb("w_hi", [P, W], F32R)
        w_lo = sb("w_lo", [P, W], F32R)
        ctx_sb = sb("ctx_sb", [P, RING, CHUNKS, D])
        ctxT = sb("ctxT", [P, K])
        scores = sb("scores", [P, K])
        probs = sb("probs", [P, K])
        probsT = sb("probsT", [P, CHUNKS, Q])
        stats1 = sb("stats1", [Q, 2, 6])
        mv1 = sb("mv1", [Q, 2, 2])
        var1 = sb("var1", [Q, 2])
        rstd1 = sb("rstd1", [Q, 2])
        xn = sb("xn", [Q, 2, D])
        qT = sb("qT", [P, 2, Q])
        power = sb("power", [Q, 1])
        rowmax = sb("rowmax", [Q, 2])
        negmax = sb("negmax", [Q, 2])
        rowsum = sb("rowsum", [Q, 4])
        recip = sb("recip", [Q, 1])
        gain = sb("gain", [Q, 1])
        attnT = sb("attnT", [P, Q])
        stats2 = sb("stats2", [Q, 2, 6])
        mv2 = sb("mv2", [Q, 2, 2])
        var2 = sb("var2", [Q, 2])
        rstd2 = sb("rstd2", [Q, 2])
        xn2 = sb("xn2", [Q, 2, D])
        xn2T = sb("xn2T", [P, Q])
        logits = sb("logits", [Q, B, E])
        pair_rows = sb("pair_rows", [Q, B, 2, ROW])
        HB = max(b1 - b0 for b0, b1 in PARTS)
        expert_i = sb("expert_i", [Q, HB, E], I32)
        expert_m = sb("expert_m", [Q, HB, E])
        tile_i = sb("tile_i", [Q, max(TILES), E], I32)
        tile_f = sb("tile_f", [Q, max(TILES), E])
        reached = sb("reached", [Q, max(TILES), E])
        lower = sb("lower", [Q, E, E])
        before = sb("before", [Q, Q])
        ones = sb("ones", [Q, Q])
        eq = sb("eq", [Q, HB, E])
        first = sb("first", [Q, HB, E])
        second = sb("second", [Q, HB, E])
        rest = sb("rest", [Q, HB, E])
        chosen = sb("chosen", [Q, HB + 1, E])
        m1 = sb("m1", [Q, HB])
        m2 = sb("m2", [Q, HB])
        idx = sb("idx", [Q, HB])
        gap = sb("gap", [Q, HB])
        ratio = sb("ratio", [Q, HB])
        euler = sb("euler", [Q, HB])
        den = sb("den", [Q, HB])
        gate1 = sb("gate1", [Q, HB])
        count_i = sb("count_i", [Q, E], I32)
        ntiles_i = sb("ntiles_i", [Q, E], I32)
        ntiles = sb("ntiles", [Q, E])
        earlier = sb("earlier", [Q, E, E])
        tile_start = sb("tile_start", [Q, E])
        tile_end = sb("tile_end", [Q, E])
        slot_base = sb("slot_base", [Q, E])
        rank_sb = sb("rank_sb", [Q, HB + 1, E])
        slot = sb("slot", [Q, HB, E])
        slot_f = sb("slot_f", [Q, HB])
        slot_i = sb("slot_i", [Q, 2, B], U32)
        tile_sum = sb("tile_sum", [Q, max(TILES)])
        tile_expert = sb("tile_expert", [Q, T], I32)
        row_in = sb("row_in", [P, RING, ROW])
        dest = sb("dest", [P, RING], U32)
        rowT_hi = sb("rowT_hi", [P, 2, P], F32R)
        rowT_lo = sb("rowT_lo", [P, 2, P], F32R)
        hidT_hi = sb("hidT_hi", [P, 2, F], F32R)
        hidT_lo = sb("hidT_lo", [P, 2, F], F32R)
        mask_rows = scores[0:B, :]
        empty = probs[:, 0:RING * ROW].rearrange("p (t w) -> p t w", w=ROW)
        silu = [probs[:, n * F:(n + 1) * F] for n in range(2)]
        hidden = [scores[:, n * F:(n + 1) * F] for n in range(2)]
        ctx_flat = ctx_sb[:, :, :, :].rearrange("p r c d -> p (r c d)")
        y_part = [ctx_flat[0:Q, p * 2 * CHUNKS * D:p * 2 * CHUNKS * D + (b1 - b0) * 2 * D].rearrange("q (b j d) -> q b j d", j=2, d=D)
                  for p, (b0, b1) in enumerate(PARTS)]

        y_sb = ctx_flat[:, 2 * HB * D:(2 * HB + RING) * D].rearrange("p (r d) -> p r d", d=D)
        assert (2 * HB + RING) * D <= 2 * CHUNKS * D

        x_first = sem("x_first")
        x_rest = sem("x_rest")
        small_loaded = sem("small_loaded")
        mask_raw = sem("mask_raw")
        mask_scaled_done = sem("mask_scaled_done")
        mask_stored = sem("mask_stored")
        mask_loaded = [sem(f"mask_loaded{s}") for s in range(2)]
        ctx_loaded = [sem(f"ctx_loaded{s}") for s in range(RING)]
        w_loaded = [sem(f"w_loaded{s}") for s in range(2)]
        w_hi_done = sem("w_hi_done")
        w_lo_done = sem("w_lo_done")
        setup = sem("setup")
        identity_done = sem("identity_done")
        empty_done = sem("empty_done")
        empty_stored = sem("empty_stored")
        tables_done = sem("tables_done")
        tanh_done = sem("tanh_done")
        stats1_done = sem("stats1_done")
        mv1_done = sem("mv1_done")
        var1_done = sem("var1_done")
        rstd1_done = sem("rstd1_done")
        xn_done = sem("xn_done")
        qT_raw = sem("qT_raw")
        qT_done = sem("qT_done")
        ctxT_raw = sem("ctxT_raw")
        ctxT_act = sem("ctxT_act")
        ctxT_dve = sem("ctxT_dve")
        scores_raw = sem("scores_raw")
        scores_done = sem("scores_done")
        negmax_done = sem("negmax_done")
        probs_done = sem("probs_done")
        probsT_raw = sem("probsT_raw")
        probsT_done = sem("probsT_done")
        attnT_raw = sem("attnT_raw")
        attnT_done = sem("attnT_done")
        attn_raw = sem("attn_raw")
        recip_done = sem("recip_done")
        gain_done = sem("gain_done")
        x2_done = sem("x2_done")
        stats2_done = sem("stats2_done")
        mv2_done = sem("mv2_done")
        var2_done = sem("var2_done")
        rstd2_done = sem("rstd2_done")
        xn2_done = sem("xn2_done")
        pairs_done = sem("pairs_done")
        xn2T_raw = sem("xn2T_raw")
        xn2T_done = sem("xn2T_done")
        logits_raw = sem("logits_raw")
        logits_done = sem("logits_done")
        route_step = sem("route_step")
        gap_done = sem("gap_done")
        ratio_done = sem("ratio_done")
        chosen_done = sem("chosen_done")
        rank_raw = sem("rank_raw")
        rank_done = sem("rank_done")
        routed = sem("routed")
        scattered = [sem(f"scattered{p}") for p in range(len(PARTS))]
        row_loaded = [sem(f"row_loaded{s}") for s in range(RING)]
        rowT_raw = sem("rowT_raw")
        rowT_hi_done = sem("rowT_hi_done")
        rowT_lo_done = sem("rowT_lo_done")
        gate_up_raw = sem("gate_up_raw")
        silu_done = sem("silu_done")
        hidden_done = sem("hidden_done")
        dest_done = sem("dest_done")
        hidT_raw = sem("hidT_raw")
        hidT_hi_done = sem("hidT_hi_done")
        hidT_lo_done = sem("hidT_lo_done")
        y_raw = sem("y_raw")
        y_done = sem("y_done")
        y_stored = [sem(f"y_stored{s}") for s in range(RING)]
        part_loaded = [sem(f"part_loaded{p}") for p in range(len(PARTS))]
        sum_done = sem("sum_done")
        out_done = sem("out_done")
        out_stored = sem("out_stored")

        def wait(eng, semaphore, value):
            if not isinstance(value, int) or value > 0:
                eng.wait_ge(semaphore, value)

        def apart(eng):
            eng.nop(nofuse=True)

        def over(eng, step, at, stop):
            assert (stop - at) % RING == 0 and at >= RING
            with eng.Fori(0, (stop - at) // RING) as i:
                for k in range(at, at + RING):
                    step(i, k)

        LOOP, LOOP_END = RING, B - RING

        def over_batches(eng, step, after=None):
            for b in range(LOOP):
                step(0, b)
            over(eng, step, LOOP, LOOP_END)
            if after:
                after(LOOP_END - 1)
            for b in range(LOOP_END, B + LAG):
                step(0, b)
                if after:
                    after(b)

        ROUTE = LOOP_END
        COMBINE = TILES[0] + 2 * RING

        def over_tiles(eng, step, after=None):
            for n in range(2 * RING):
                step(0, n)
                if after:
                    after(n)
            over(eng, step, 2 * RING, COMBINE)
            if after:
                after(COMBINE - 1)
            over(eng, step, COMBINE, T - RING)
            for n in range(T - RING, T + 2):
                step(0, n)

        block = stack.enter_context(nc.Block())

        @block.sync
        def _(sp):
            def load_ctx(i, k):
                b = i * RING + k
                s = k % RING
                sp.dma_start(ctx_sb[0:full, s, :, :],
                             ctx[b, 0:full * CHUNKS, :].rearrange("(p c) d -> p c d", c=CHUNKS)).then_inc(ctx_loaded[s], 16)
                sp.dma_start(ctx_sb[full:full + 1, s, 0:extra, :],
                             ctx[b, full * CHUNKS:K, :].rearrange("(p c) d -> p c d", p=1)).then_inc(ctx_loaded[s], 16)

            def load_mask(i, k):
                sp.dma_start(maskb[:, k % 2, :], mask_scaled[i * RING + k, :].partition_broadcast(Q)).then_inc(mask_loaded[k % 2], 16)

            def load_weights(i, k):
                b = i * RING + k
                wait(sp, w_lo_done, b - 1)
                sp.dma_start(w_raw[:, k % 2, :], w_experts[:, bass.ds(b * WC, WC)]).then_inc(w_loaded[k % 2], 16)

            sp.dma_start(mask_rows, mask).then_inc(mask_raw, 16)
            sp.dma_start(x_all[:, 0:1, :], x[0:1, :, :].rearrange("b q d -> q b d")).then_inc(x_first, 16)
            load_ctx(0, 0)
            sp.dma_start(x_all[:, 1:B, :], x[1:B, :, :].rearrange("b q d -> q b d")).then_inc(x_rest, 16)
            sp.wait_ge(mask_scaled_done, 1)
            sp.dma_start(mask_scaled, mask_rows).then_inc(mask_stored, 16)
            load_ctx(0, 1)
            sp.wait_ge(mask_stored, 16)
            load_mask(0, 0)
            load_mask(0, 1)
            load_weights(0, 0)
            load_ctx(0, 2)
            sp.wait_ge(empty_done, 1)
            for t in range(0, T, RING):
                sp.dma_start(slots[t * P:(t + RING) * P, :].rearrange("(t p) w -> p t w", p=P), empty).then_inc(empty_stored, 16)
            load_weights(0, 1)
            load_ctx(0, 3)

            def step(i, k):
                b = i * RING + k
                sp.wait_ge(scores_done, b + 1)
                if k + 2 < B:
                    load_mask(i, k + 2)
                    load_weights(i, k + 2)
                if k + RING < B:
                    sp.wait_ge(attnT_raw, b + 1)
                    load_ctx(i, k + RING)

            with sp.Fori(0, (B - RING) // RING) as i:
                for k in range(RING):
                    step(i, k)
            for k in range(B - RING, B - 2):
                step(0, k)

            def load_rows(i, k):
                n = i * RING + k
                wait(sp, hidden_done, n - RING + 1)
                sp.dma_start(row_in[:, k % RING, :], slots[bass.ds(n * P, P), :]).then_inc(row_loaded[k % RING], 16)

            def load_part(p):
                b0, b1 = PARTS[p]
                done = sum(TILES[:p + 1])
                for s in range(RING):
                    sp.wait_ge(y_stored[s], 16 * (done // RING))
                sp.dma_start(y_part[p], results[2 * Q * b0:2 * Q * b1, :].rearrange("(b q j) d -> q b j d", q=Q, j=2)).then_inc(part_loaded[p], 16)

            def store_part(p):
                b0, b1 = PARTS[p]
                sp.wait_ge(out_done, p + 1)
                sp.dma_start(out[b0:b1, :, :].rearrange("b q d -> q b d"), x_all[:, b0:b1, :]).then_inc(out_stored, 16)

            sp.wait_ge(scattered[0], 16 * 2 * (PARTS[0][1] - PARTS[0][0]))
            for k in range(RING):
                load_rows(0, k)
            over(sp, load_rows, RING, TILES[0])
            sp.wait_ge(scattered[1], 16 * 2 * (PARTS[1][1] - PARTS[1][0]))
            over(sp, load_rows, TILES[0], COMBINE)
            load_part(0)
            over(sp, load_rows, COMBINE, T)
            store_part(0)
            load_part(1)
            store_part(1)
            sp.wait_ge(out_stored, 16 * len(PARTS))

        @block.gpsimd
        def _(pool):
            made = [0]

            def link(ins):
                made[0] += 1
                ins.then_inc(setup, 1)
                pool.wait_ge(setup, made[0])

            nc.gpsimd.memset(power[:, :], -0.5)
            link(nc.gpsimd.memset(identity[:, :], 0.0))
            nc.gpsimd.affine_select(out=identity[:, :], in_=identity[:, :], compare_op=ALU.not_equal, fill=1.0,
                                    base=0, pattern=[[-1, P]], channel_multiplier=1).then_inc(identity_done, 1)
            link(nc.gpsimd.memset(empty, 0.0))
            nc.gpsimd.iota(empty[:, :, D + 1:D + 2].bitcast(I32), pattern=[[P, RING], [1, 1]], base=PAIRS,
                           channel_multiplier=1).then_inc(empty_done, 1)

            def tables():
                nc.gpsimd.memset(euler[:, :], EULER)
                nc.gpsimd.memset(before[:, :], 1.0)
                nc.gpsimd.memset(lower[:, :, :], 1.0)
                nc.gpsimd.memset(chosen[:, :, :], 0.0)
                link(nc.gpsimd.memset(ones[:, :], 1.0))
                nc.gpsimd.affine_select(out=before[:, :], in_=before[:, :], compare_op=ALU.is_gt, fill=0.0,
                                        base=0, pattern=[[1, Q]], channel_multiplier=-1)
                nc.gpsimd.affine_select(out=lower[:, :, :], in_=lower[:, :, :], compare_op=ALU.is_gt, fill=0.0,
                                        base=0, pattern=[[1, E], [-1, E]], channel_multiplier=0)
                nc.gpsimd.iota(expert_i[:, :, :], pattern=[[0, HB], [1, E]], base=-E, channel_multiplier=0)
                nc.gpsimd.iota(tile_i[:, :, :], pattern=[[1, max(TILES)], [0, E]], base=0, channel_multiplier=0)
                link(nc.gpsimd.iota(pair_rows[:, :, :, D + 1:D + 2].bitcast(I32), pattern=[[2 * Q, B], [1, 2], [1, 1]],
                                    base=0, channel_multiplier=2))
                nc.gpsimd.tensor_copy(expert_m[:, :, :], expert_i[:, :, :])
                nc.gpsimd.tensor_copy(tile_f[:, :, :], tile_i[:, :, :]).then_inc(tables_done, 1)

            def inverse_root(i, k, mv, var, rstd, mv_done, var_done, rstd_done):
                b = i * RING + k
                s = k % 2
                pool.wait_ge(mv_done, b + 1)
                apart(pool)
                nc.gpsimd.tensor_scalar(var[:, s:s + 1], mv[:, s, 1:2], EPS, None, ALU.add).then_inc(var_done, 1)
                pool.wait_ge(var_done, b + 1)
                nc.gpsimd.tensor_tensor(rstd[:, s:s + 1], var[:, s:s + 1], power[:, :], ALU.pow).then_inc(rstd_done, 1)

            def root1(i, k):
                inverse_root(i, k, mv1, var1, rstd1, mv1_done, var1_done, rstd1_done)

            def root2(i, k):
                inverse_root(i, k, mv2, var2, rstd2, mv2_done, var2_done, rstd2_done)

            def copy_pairs(i, k):
                b = i * RING + k
                pool.wait_ge(xn2_done, b + 1)
                apart(pool)
                nc.gpsimd.tensor_copy(pair_rows[:, b, :, 0:D],
                                      xn2[:, k % 2, :].unsqueeze(1).to_broadcast([Q, 2, D])).then_inc(pairs_done, 1)

            def split_weights(i, k):
                b = i * RING + k
                pool.wait_ge(w_hi_done, b + 1)
                apart(pool)
                nc.gpsimd.tensor_tensor(w_lo[:, bass.ds(b * WC, WC)], w_raw[:, k % 2, :],
                                        w_hi[:, bass.ds(b * WC, WC)].bitcast(F32), ALU.subtract).then_inc(w_lo_done, 1)

            def step(i, k):
                if 0 <= k - LAG < B:
                    copy_pairs(i, k - LAG)
                if k < B:
                    split_weights(i, k)
                if k - 2 >= 0 and k - 2 < B:
                    root2(i, k - 2)
                if k + 2 < B:
                    root1(i, k + 2)

            def scatter(p, j, b):
                nc.gpsimd.indirect_dma_start(slots, bass.IndirectOffsetOnAxis(ap=slot_i[:, j, b:b + 1], axis=0),
                                             pair_rows[:, b, j, :], None).then_inc(scattered[p], 16)

            def ratios(p):
                n = PARTS[p][1] - PARTS[p][0]
                pool.wait_ge(gap_done, p + 1)
                nc.gpsimd.tensor_tensor(ratio[:, 0:n], euler[:, 0:n], gap[:, 0:n], ALU.pow).then_inc(ratio_done, 1)

            pending = [(0, j, b) for b in range(*PARTS[0]) for j in range(2)]

            def after(b):
                if b == ROUTE - 1:
                    ratios(0)
                if b > ROUTE:
                    if b == ROUTE + 1:
                        pool.wait_ge(routed, 1)
                        pool.wait_ge(empty_stored, 16 * (T // RING))
                    for _ in range(5 if b < B - 1 else 16):
                        if pending:
                            scatter(*pending.pop(0))

            root1(0, 0)
            root1(0, 1)
            tables()
            over_batches(pool, step, after)

            def scatter_result(i, k):
                n = i * RING + k
                s = k % RING
                pool.wait_ge(y_done, n + 1)
                pool.wait_ge(dest_done, n + 1)
                apart(pool)
                nc.gpsimd.indirect_dma_start(results, bass.IndirectOffsetOnAxis(ap=dest[:, s:s + 1], axis=0),
                                             y_sb[:, s, :], None).then_inc(y_stored[s], 16)

            ratios(1)
            pool.wait_ge(routed, 2)
            pending = [(1, j, b) for b in range(*PARTS[1]) for j in range(2)]
            for n in range(2 * RING):
                scatter_result(0, n)
                for _ in range(2):
                    scatter(*pending.pop(0))
            over(pool, scatter_result, 2 * RING, T)

        @block.scalar
        def _(act):
            act.dma_start(wi_col[:, :], w_input.rearrange("o d -> d o")).then_inc(small_loaded, 16)
            act.dma_start(ds_col[:, :], dot_scale.rearrange("(d o) -> d o", o=1)).then_inc(small_loaded, 16)
            act.dma_start(gates_in[:, 0:1], g_xattn.partition_broadcast(P)).then_inc(small_loaded, 16)
            act.dma_start(gates_in[:, 1:2], g_ffn.partition_broadcast(P)).then_inc(small_loaded, 16)
            act.dma_start(wr_sb[:, :], w_router).then_inc(small_loaded, 16)
            act.wait_ge(small_loaded, 80)
            nc.scalar.activation(tanh_g[:, :], gates_in[:, :], ACT.Tanh).then_inc(tanh_done, 1)

            def ctxT_first(i, k):
                b = i * RING + k
                act.wait_ge(ctxT_raw, b * GROUPS + 1)
                nc.scalar.activation(ctxT[:, 0:group_start[1]], ring_ps[0][:, 0:group_start[1]],
                                     ACT.Identity, bias=wi_col[:, 0:1], scale=ds_col[:, 0:1]).then_inc(ctxT_act, 1)

            def copy_qT(i, k):
                b = i * RING + k
                act.wait_ge(qT_raw, b + 1)
                nc.scalar.activation(qT[:, k % 2, :], ring_ps[0][:, GROUP * Q:GROUP * Q + Q], ACT.Copy).then_inc(qT_done, 1)

            def copy_probsT(i, k, g):
                b = i * RING + k
                act.wait_ge(probsT_raw, b * GROUPS + g + 1)
                n = rows[g * GROUP]
                nc.scalar.activation(probsT[0:n, g * GROUP:(g + 1) * GROUP, :],
                                     ring_ps[g][0:n, 0:GROUP * Q].rearrange("p (c q) -> p c q", c=GROUP),
                                     ACT.Copy).then_inc(probsT_done, 1)

            def step(i, k):
                b = i * RING + k
                if 0 <= k - 2 < B:
                    act.wait_ge(attnT_raw, b - 1)
                    nc.scalar.activation(attnT[:, :], attn_ps[:, 0:Q], ACT.Copy).then_inc(attnT_done, 1)
                if 0 <= k - 1 < B:
                    if k + 1 < B:
                        act.wait_ge(probsT_raw, (b - 1) * GROUPS + 1)
                        copy_qT(i, k + 1)
                    for g in range(GROUPS):
                        copy_probsT(i, k - 1, g)
                elif k == 0:
                    copy_qT(0, 1)
                if 0 <= k - LAG < B:
                    act.wait_ge(xn2T_raw, b - LAG + 1)
                    nc.scalar.activation(xn2T[:, :], router_ps[:, 0:Q], ACT.Copy).then_inc(xn2T_done, 1)
                if k + 1 < B:
                    ctxT_first(i, k + 1)
                if k < B:
                    act.wait_ge(w_loaded[k % 2], i * (16 * RING // 2) + 16 * (k // 2 + 1))
                    apart(act)
                    nc.scalar.activation(w_hi[:, bass.ds(b * WC, WC)], w_raw[:, k % 2, :], ACT.Copy).then_inc(w_hi_done, 1)
                    act.wait_ge(negmax_done, b + 1)
                    if k == 0:
                        act.wait_ge(empty_stored, 16 * (T // RING))
                    nc.scalar.activation(probs[0:Q, :], scores[0:Q, :], ACT.Exp, bias=negmax[:, k % 2:k % 2 + 1],
                                         accum_out=rowsum[:, k % RING:k % RING + 1]).then_inc(probs_done, 1)

            copy_qT(0, 0)
            ctxT_first(0, 0)
            over_batches(act, step)

            def rowT_high(i, k):
                n = i * RING + k
                act.wait_ge(rowT_raw, n + 1)
                nc.scalar.activation(rowT_hi[:, k % 2, :], rowT_ps, ACT.Copy).then_inc(rowT_hi_done, 1)

            def tile_step(i, k):
                n = i * RING + k
                if k + 1 < T:
                    rowT_high(i, k + 1)
                if k < T:
                    act.wait_ge(gate_up_raw, n + 1)
                    wait(act, hidden_done, n - 1)
                    nc.scalar.activation(silu[k % 2], gate_ps[k % 2], ACT.Silu).then_inc(silu_done, 1)
                if 0 <= k - 1 < T:
                    act.wait_ge(hidT_raw, n)
                    nc.scalar.activation(hidT_hi[:, (k - 1) % 2, :], hidT_ps, ACT.Copy).then_inc(hidT_hi_done, 1)
                if k - 2 >= 0:
                    s = (k - 2) % RING
                    act.wait_ge(y_raw, n - 1)
                    wait(act, y_stored[s], i * 16 + 16 * ((k - 2) // RING))
                    nc.scalar.activation(y_sb[:, s, :], y_ps, ACT.Copy).then_inc(y_done, 1)

            rowT_high(0, 0)
            over_tiles(act, tile_step)

        @block.vector
        def _(dve):
            dve.wait_ge(mask_raw, 16)
            nc.vector.tensor_scalar(mask_rows, mask_rows, NEG, None, ALU.mult).then_inc(mask_scaled_done, 1)

            def statistics1(i, k):
                b = i * RING + k
                s = k % 2
                dve.wait_ge(x_first if k == 0 else x_rest, 16)
                nc.vector.bn_stats(stats1[:, s, :], x_all[:, b, :]).then_inc(stats1_done, 1)
                dve.wait_ge(stats1_done, b + 1)
                apart(dve)
                nc.vector.bn_aggr(mv1[:, s, :], stats1[:, s, :]).then_inc(mv1_done, 1)

            def normalise1(i, k):
                b = i * RING + k
                s = k % 2
                dve.wait_ge(rstd1_done, b + 1)
                nc.vector.tensor_scalar(xn[:, s, :], x_all[:, b, :], mv1[:, s, 0:1], rstd1[:, s:s + 1],
                                        ALU.subtract, ALU.mult).then_inc(xn_done, 1)

            def ctxT_rest(i, k, g):
                b = i * RING + k
                dve.wait_ge(ctxT_raw, b * GROUPS + g + 1)
                n = group_start[g + 1] - group_start[g]
                nc.vector.tensor_scalar(ctxT[:, group_start[g]:group_start[g + 1]], ring_ps[g][:, 0:n],
                                        ds_col[:, 0:1], wi_col[:, 0:1], ALU.mult, ALU.add).then_inc(ctxT_dve, 1)

            def attention_gain(i, k):
                b = i * RING + k
                dve.wait_ge(probs_done, b + 1)
                nc.vector.reciprocal(recip[:, :], rowsum[:, k % RING:k % RING + 1]).then_inc(recip_done, 1)
                dve.wait_ge(recip_done, b + 1)
                nc.vector.tensor_scalar(gain[:, :], recip[:, :], tanh_g[0:Q, 0:1], None, ALU.mult).then_inc(gain_done, 1)

            def residual(i, k):
                b = i * RING + k
                dve.wait_ge(gain_done, b + 1)
                dve.wait_ge(attn_raw, b + 1)
                nc.vector.scalar_tensor_tensor(out=x_all[:, b, :], in0=attn_ps[0:Q, P:P + D], scalar=gain[:, :],
                                               in1=x_all[:, b, :], op0=ALU.mult, op1=ALU.add).then_inc(x2_done, 1)

            def statistics2(i, k):
                b = i * RING + k
                s = k % 2
                dve.wait_ge(x2_done, b + 1)
                apart(dve)
                nc.vector.bn_stats(stats2[:, s, :], x_all[:, b, :]).then_inc(stats2_done, 1)
                dve.wait_ge(stats2_done, b + 1)
                apart(dve)
                nc.vector.bn_aggr(mv2[:, s, :], stats2[:, s, :]).then_inc(mv2_done, 1)

            def step(i, k):
                b = i * RING + k
                s = slice(k % 2, k % 2 + 1)
                if 0 <= k - LAG < B:
                    o = (k - LAG) % 2
                    dve.wait_ge(rstd2_done, b - LAG + 1)
                    nc.vector.tensor_scalar(xn2[:, o, :], x_all[:, b - LAG, :], mv2[:, o, 0:1], rstd2[:, o:o + 1],
                                            ALU.subtract, ALU.mult).then_inc(xn2_done, 1)
                if k + 1 < B:
                    normalise1(i, k + 1)
                if 0 <= k - 2 < B:
                    attention_gain(i, k - 2)
                if k < B:
                    dve.wait_ge(scores_raw, b + 1)
                    dve.wait_ge(mask_loaded[k % 2], i * (16 * RING // 2) + 16 * (k // 2 + 1))
                    wait(dve, probs_done, b)
                    apart(dve)
                    nc.vector.tensor_tensor_reduce(out=scores[0:Q, :], in0=scores_ps[0:Q, 0:K], in1=maskb[:, k % 2, :],
                                                   scale=1.0, scalar=LOWEST, op0=ALU.add, op1=ALU.max,
                                                   accum_out=rowmax[:, s]).then_inc(scores_done, 1)
                    dve.wait_ge(scores_done, b + 1)
                    nc.vector.tensor_scalar(negmax[:, s], rowmax[:, s], -1.0, None, ALU.mult).then_inc(negmax_done, 1)
                if 0 <= k - 2 < B:
                    residual(i, k - 2)
                if k + 1 < B:
                    ctxT_rest(i, k + 1, 1)
                    ctxT_rest(i, k + 1, 2)
                if 0 <= k - 2 < B:
                    statistics2(i, k - 2)
                if k + 2 < B:
                    statistics1(i, k + 2)
                if 0 <= k - LAG < B:
                    dve.wait_ge(logits_raw, b - LAG + 1)
                    nc.vector.tensor_copy(logits[:, b - LAG, :], router_ps[0:Q, P:P + E]).then_inc(logits_done, 1)

            linked = [0]

            def link(ins):
                linked[0] += 1
                ins.then_inc(route_step, 1)
                dve.wait_ge(route_step, linked[0])

            def choose(p):
                b0, b1 = PARTS[p]
                n = b1 - b0
                part = logits[:, b0:b1, :]

                def wide(a):
                    return a[:, 0:n].unsqueeze(2).to_broadcast([Q, n, E])

                def pick(values, top, choice):
                    link(nc.vector.tensor_reduce(top[:, 0:n], values, axis=X, op=ALU.max))
                    link(nc.vector.tensor_tensor(eq[:, 0:n, :], values, wide(top), ALU.is_equal))
                    link(nc.vector.tensor_tensor(eq[:, 0:n, :], eq[:, 0:n, :], expert_m[:, 0:n, :], ALU.mult))
                    link(nc.vector.tensor_reduce(idx[:, 0:n], eq[:, 0:n, :], axis=X, op=ALU.min))
                    link(nc.vector.tensor_tensor(choice[:, 0:n, :], expert_m[:, 0:n, :], wide(idx), ALU.is_equal))

                dve.wait_ge(logits_done, b1)
                dve.wait_ge(tables_done, 1)
                if p > 0:
                    dve.wait_ge(rank_raw, p)
                pick(part, m1, first)
                link(nc.vector.scalar_tensor_tensor(out=rest[:, 0:n, :], in0=first[:, 0:n, :], scalar=LOWEST, in1=part,
                                                    op0=ALU.mult, op1=ALU.add))
                pick(rest[:, 0:n, :], m2, second)
                nc.vector.tensor_tensor(chosen[:, 0:n, :], first[:, 0:n, :], second[:, 0:n, :], ALU.add).then_inc(chosen_done, 1)
                nc.vector.tensor_tensor(gap[:, 0:n], m2[:, 0:n], m1[:, 0:n], ALU.subtract).then_inc(gap_done, 1)

            def place(p):
                b0, b1 = PARTS[p]
                n = b1 - b0
                nt = TILES[p]
                dve.wait_ge(ratio_done, p + 1)
                link(nc.vector.tensor_scalar(den[:, 0:n], ratio[:, 0:n], 1.0, None, ALU.add))
                link(nc.vector.reciprocal(gate1[:, 0:n], den[:, 0:n]))
                link(nc.vector.tensor_copy(pair_rows[:, b0:b1, 0, D:D + 1], gate1[:, 0:n].unsqueeze(2)))
                link(nc.vector.tensor_tensor(pair_rows[:, b0:b1, 1, D:D + 1], gate1[:, 0:n].unsqueeze(2),
                                             ratio[:, 0:n].unsqueeze(2), ALU.mult))
                dve.wait_ge(rank_raw, p + 1)
                rank = rank_sb[:, 0:n + 1, :]
                nc.vector.tensor_copy(rank, router_ps[0:Q, 2 * P:2 * P + (n + 1) * E].rearrange("q (b e) -> q b e", e=E)
                                      ).then_inc(rank_done, 1)
                dve.wait_ge(rank_done, p + 1)
                link(nc.vector.tensor_scalar(count_i[:, :], rank[:, n, :], float(P - 1), None, ALU.add))
                link(nc.vector.tensor_scalar(ntiles_i[:, :], count_i[:, :], 7, None, ALU.logical_shift_right))
                link(nc.vector.tensor_copy(ntiles[:, :], ntiles_i[:, :]))
                link(nc.vector.tensor_tensor(earlier[:, :, :], lower[:, :, :],
                                             ntiles[:, :].unsqueeze(1).to_broadcast([Q, E, E]), ALU.mult))
                link(nc.vector.tensor_reduce(tile_start[:, :], earlier[:, :, :], axis=X, op=ALU.add))
                link(nc.vector.tensor_tensor(tile_end[:, :], tile_start[:, :], ntiles[:, :], ALU.add))
                link(nc.vector.tensor_scalar(slot_base[:, :], tile_start[:, :], float(P), float(SLOT0[p]), ALU.mult, ALU.add))
                link(nc.vector.tensor_tensor(slot[:, 0:n, :], rank[:, 0:n, :],
                                             slot_base[:, :].unsqueeze(1).to_broadcast([Q, n, E]), ALU.add))
                for j, choice in enumerate((first, second)):
                    link(nc.vector.tensor_tensor(eq[:, 0:n, :], choice[:, 0:n, :], slot[:, 0:n, :], ALU.mult))
                    link(nc.vector.tensor_reduce(slot_f[:, 0:n], eq[:, 0:n, :], axis=X, op=ALU.add))
                    link(nc.vector.tensor_copy(slot_i[:, j, b0:b1], slot_f[:, 0:n]))
                link(nc.vector.tensor_tensor(reached[:, 0:nt, :], tile_f[:, 0:nt, :],
                                             tile_end[:, :].unsqueeze(1).to_broadcast([Q, nt, E]), ALU.is_ge))
                link(nc.vector.tensor_reduce(tile_sum[:, 0:nt], reached[:, 0:nt, :], axis=X, op=ALU.add))
                t0 = sum(TILES[:p])
                dve.wait_ge(pairs_done, b1)
                nc.vector.tensor_scalar(tile_expert[:, t0:t0 + nt], tile_sum[:, 0:nt], float(E - 1), None,
                                        ALU.min).then_inc(routed, 1)

            def after(b):
                if b == ROUTE - 1:
                    choose(0)
                if b == ROUTE:
                    place(0)

            statistics1(0, 0)
            statistics1(0, 1)
            normalise1(0, 0)
            dve.wait_ge(small_loaded, 80)
            dve.wait_ge(tanh_done, 1)
            ctxT_rest(0, 0, 1)
            ctxT_rest(0, 0, 2)
            over_batches(dve, step, after)

            def rowT_low(i, k):
                n = i * RING + k
                dve.wait_ge(rowT_hi_done, n + 1)
                nc.vector.tensor_tensor(rowT_lo[:, k % 2, :], rowT_ps, rowT_hi[:, k % 2, :].bitcast(F32),
                                        ALU.subtract).then_inc(rowT_lo_done, 1)

            def tile_step(i, k):
                n = i * RING + k
                if k + 1 < T:
                    rowT_low(i, k + 1)
                if k < T:
                    s = k % RING
                    wait(dve, y_stored[s], i * 16 + 16 * (k // RING))
                    nc.vector.tensor_copy(dest[:, s:s + 1], row_in[:, s, D + 1:D + 2].bitcast(U32)).then_inc(dest_done, 1)
                    dve.wait_ge(silu_done, n + 1)
                    wait(dve, hidT_raw, n - 1)
                    nc.vector.scalar_tensor_tensor(out=hidden[k % 2], in0=silu[k % 2], scalar=row_in[:, s, D:D + 1],
                                                   in1=up_ps[k % 2], op0=ALU.mult, op1=ALU.mult).then_inc(hidden_done, 1)
                if 0 <= k - 1 < T:
                    dve.wait_ge(hidT_hi_done, n)
                    nc.vector.tensor_tensor(hidT_lo[:, (k - 1) % 2, :], hidT_ps, hidT_hi[:, (k - 1) % 2, :].bitcast(F32),
                                            ALU.subtract).then_inc(hidT_lo_done, 1)

            def combine(p):
                b0, b1 = PARTS[p]
                y = y_part[p]
                dve.wait_ge(part_loaded[p], 16)
                nc.vector.tensor_tensor(y[:, :, 0, :], y[:, :, 0, :], y[:, :, 1, :], ALU.add).then_inc(sum_done, 1)
                dve.wait_ge(sum_done, p + 1)
                nc.vector.scalar_tensor_tensor(out=x_all[:, b0:b1, :], in0=y[:, :, 0, :], scalar=tanh_g[0:Q, 1:2],
                                               in1=x_all[:, b0:b1, :], op0=ALU.mult, op1=ALU.add).then_inc(out_done, 1)

            def between(n):
                if n == 0:
                    place(1)
                if n == COMBINE - 1:
                    combine(0)

            choose(1)
            rowT_low(0, 0)
            over_tiles(dve, tile_step, between)
            combine(1)

        @block.tensor
        def _(pe):
            pe.wait_ge(identity_done, 1)

            def transpose_q(i, k):
                b = i * RING + k
                pe.wait_ge(xn_done, b + 1)
                nc.tensor.transpose(ring_ps[0][:, GROUP * Q:GROUP * Q + Q], xn[:, k % 2, :],
                                    identity[0:Q, 0:Q]).then_inc(qT_raw, 1)

            def transpose_ctx(i, k):
                b = i * RING + k
                s = k % RING
                pe.wait_ge(ctx_loaded[s], i * 32 + 32 * (k // RING + 1))
                for g in range(GROUPS):
                    if k == 0:
                        pe.wait_ge(qT_done, 1)
                    elif k == 1:
                        pe.wait_ge(qT_done, 2)
                        if g > 0:
                            pe.wait_ge(ctxT_dve, 2)
                    else:
                        pe.wait_ge(probsT_done, (b - 2) * GROUPS + g + 1)
                    for c in range(g * GROUP, (g + 1) * GROUP):
                        at = starts[c] - group_start[g]
                        last = nc.tensor.transpose(ring_ps[g][:, at:at + rows[c]],
                                                   ctx_sb[0:rows[c], s, c, :], identity[0:rows[c], 0:rows[c]])
                    last.then_inc(ctxT_raw, 1)

            def score(i, k):
                b = i * RING + k
                pe.wait_ge(qT_done, b + 1)
                pe.wait_ge(ctxT_act, b + 1)
                pe.wait_ge(ctxT_dve, 2 * b + 2)
                wait(pe, scores_done, b)
                for n in range(0, K, 512):
                    m = min(512, K - n)
                    last = nc.tensor.matmul(scores_ps[0:Q, n:n + m], qT[:, k % 2, :], ctxT[:, n:n + m], start=True, stop=True)
                last.then_inc(scores_raw, 1)

            def transpose_attn(i, k):
                b = i * RING + k
                pe.wait_ge(attnT_done, b + 1)
                nc.tensor.transpose(attn_ps[0:Q, P:P + D], attnT[:, :], identity[:, :]).then_inc(attn_raw, 1)

            def transpose_probs(i, k, q_too):
                b = i * RING + k
                pe.wait_ge(probs_done, b + 1)
                for g in range(GROUPS):
                    if g == 0 and q_too:
                        transpose_q(i, k + 2)
                    for c in range(g * GROUP, (g + 1) * GROUP):
                        at = (c - g * GROUP) * Q
                        last = nc.tensor.transpose(ring_ps[g][0:rows[c], at:at + Q],
                                                   probs[0:Q, starts[c]:starts[c] + rows[c]], identity[0:Q, 0:Q])
                    last.then_inc(probsT_raw, 1)

            def attend(i, k):
                b = i * RING + k
                wait(pe, x2_done, b)
                for g in range(GROUPS):
                    pe.wait_ge(probsT_done, b * GROUPS + g + 1)
                    for c in range(g * GROUP, (g + 1) * GROUP):
                        last = nc.tensor.matmul(attn_ps[:, 0:Q], ctx_sb[0:rows[c], k % RING, c, :], probsT[0:rows[c], c, :],
                                                start=(c == 0), stop=(c == CHUNKS - 1))
                last.then_inc(attnT_raw, 1)

            def step(i, k):
                b = i * RING + k
                if k < B:
                    score(i, k)
                if 0 <= k - 2 < B:
                    transpose_attn(i, k - 2)
                if 0 <= k - 1 < B:
                    transpose_probs(i, k - 1, k + 1 < B)
                elif k == 0:
                    pe.wait_ge(ctxT_act, 1)
                    transpose_q(0, 1)
                if 0 <= k - LAG < B:
                    wait(pe, logits_done, b - LAG)
                    if k == ROUTE + 1:
                        pe.wait_ge(rank_done, 1)
                    pe.wait_ge(xn2_done, b - LAG + 1)
                    nc.tensor.transpose(router_ps[:, 0:Q], xn2[:, (k - LAG) % 2, :], identity[0:Q, 0:Q]).then_inc(xn2T_raw, 1)
                if k + 1 < B:
                    transpose_ctx(i, k + 1)
                if 0 <= k - LAG < B:
                    pe.wait_ge(xn2T_done, b - LAG + 1)
                    nc.tensor.matmul(router_ps[0:Q, P:P + E], xn2T[:, :], wr_sb[:, :], start=True, stop=True).then_inc(logits_raw, 1)
                if k == ROUTE:
                    ranks(0, ROUTE - LAG + 1)
                if 0 <= k - 1 < B:
                    attend(i, k - 1)

            def ranks(p, logits_out):
                n = PARTS[p][1] - PARTS[p][0]
                pe.wait_ge(logits_done, logits_out)
                pe.wait_ge(chosen_done, p + 1)
                at = 2 * P
                end = at + (n + 1) * E
                nc.tensor.matmul(router_ps[0:Q, at:end], before[:, :], chosen[:, 0:n + 1, :].rearrange("q b e -> q (b e)"),
                                 start=True, stop=False, skip_group_check=True)
                for d in range(1, n + 1):
                    last = nc.tensor.matmul(router_ps[0:Q, at + d * E:end], ones[:, :],
                                            chosen[:, 0:n + 1 - d, :].rearrange("q b e -> q (b e)"),
                                            start=False, stop=(d == n), skip_group_check=True)
                last.then_inc(rank_raw, 1)

            transpose_q(0, 0)
            transpose_ctx(0, 0)
            over_batches(pe, step)

            def transpose_rows(i, k):
                n = i * RING + k
                pe.wait_ge(row_loaded[k % RING], i * 16 + 16 * (k // RING + 1))
                wait(pe, rowT_lo_done, n)
                nc.tensor.transpose(rowT_ps, row_in[:, k % RING, 0:D], identity[:, :]).then_inc(rowT_raw, 1)

            def gate_up(i, k):
                n = i * RING + k
                o = k % 2
                e = pe.value_load(tile_expert[0:1, bass.ds(n, 1)], min_val=0, max_val=E - 1)
                pe.wait_ge(rowT_lo_done, n + 1)
                wait(pe, hidden_done, n - 1)
                for ps, col in ((gate_ps[o], 0), (up_ps[o], UP)):
                    hi, lo = (w[:, bass.ds(e * F + col, F)] for w in (w_hi, w_lo))
                    nc.tensor.matmul(ps, rowT_hi[:, o, :], hi, start=True, stop=False)
                    nc.tensor.matmul(ps, rowT_hi[:, o, :], lo, start=False, stop=False)
                    last = nc.tensor.matmul(ps, rowT_lo[:, o, :], hi, start=False, stop=True)
                last.then_inc(gate_up_raw, 1)

            def transpose_hidden(i, k):
                n = i * RING + k
                pe.wait_ge(hidden_done, n + 1)
                wait(pe, hidT_lo_done, n)
                for c in range(FC):
                    last = nc.tensor.transpose(hidT_ps[:, c * P:(c + 1) * P], hidden[k % 2][:, c * P:(c + 1) * P], identity[:, :])
                last.then_inc(hidT_raw, 1)

            def down(i, k):
                n = i * RING + k
                o = k % 2
                e = pe.value_load(tile_expert[0:1, bass.ds(n, 1)], min_val=0, max_val=E - 1)
                pe.wait_ge(hidT_lo_done, n + 1)
                wait(pe, y_done, n)
                for c in range(FC):
                    hi, lo = (w[:, bass.ds(e * F + (DOWN + c * P), P)] for w in (w_hi, w_lo))
                    at = slice(c * P, (c + 1) * P)
                    nc.tensor.matmul(y_ps, hidT_hi[:, o, at], hi, start=(c == 0), stop=False)
                    nc.tensor.matmul(y_ps, hidT_hi[:, o, at], lo, start=False, stop=False)
                    last = nc.tensor.matmul(y_ps, hidT_lo[:, o, at], hi, start=False, stop=(c == FC - 1))
                last.then_inc(y_raw, 1)

            def tile_step(i, k):
                if k + 1 < T:
                    transpose_rows(i, k + 1)
                if k < T:
                    gate_up(i, k)
                if 0 <= k - 1 < T:
                    transpose_hidden(i, k - 1)
                if k - 2 >= 0:
                    down(i, k - 2)

            def between(n):
                if n == 0:
                    ranks(1, B)

            pe.wait_ge(w_lo_done, B)
            pe.wait_ge(routed, 1)
            transpose_rows(0, 0)
            over_tiles(pe, tile_step, between)


_IN = ["x", "ctx", "mask", "g_xattn", "g_ffn", "w_input", "dot_scale", "w_router", "w_experts"]


def kernel(**inputs):
    import numpy as np
    import concourse.bacc as bacc
    from concourse.bass_utils import run_bass_kernel_spmd

    a = {k: np.asarray(v) for k, v in inputs.items()}
    mask = a["mask_BxS2_fk0"]
    K = mask.shape[1]
    rows, _ = key_order(K)
    order = np.concatenate([np.arange(rows[c]) * CHUNKS + c for c in range(CHUNKS)])
    E, F, D = a["L0_ffn_W_gate"].shape
    laid = {
        "x": a["x"],
        "ctx": a["ctx_1024"],
        "mask": mask[:, order],
        "g_xattn": a["g_xattn"],
        "g_ffn": a["g_ffn"],
        "w_input": a["L0_xattn_w_input"],
        "dot_scale": a["L0_xattn_dot_scale"],
        "w_router": a["L0_ffn_W_router"].T,
        "w_experts": np.concatenate([
            a["L0_ffn_W_gate"].transpose(2, 0, 1).reshape(D, E * F),
            a["L0_ffn_W_up"].transpose(2, 0, 1).reshape(D, E * F),
            a["L0_ffn_W_down"].reshape(E, D, F // P, P).transpose(3, 0, 2, 1).reshape(P, E * F)], axis=1),
    }
    nc = bacc.Bacc("TRN2", target_bir_lowering=False, num_devices=1)
    arrays, args = {}, []
    for name in _IN:
        v = np.ascontiguousarray(laid[name])
        arrays[f"in_{name}"] = v
        args.append(nc.dram_tensor(f"in_{name}", v.shape, mybir.dt.from_np(v.dtype), kind="ExternalInput").ap())
    out = nc.dram_tensor("out_0", a["x"].shape, F32, kind="ExternalOutput").ap()
    build(nc, *args, out)
    r = run_bass_kernel_spmd(nc, [arrays], core_ids=[0])
    return r.results[0]["out_0"]
```
